# Optimizing a Trainium2 kernel written in Bass

```python
import numpy as np
import jax
import jax.numpy as jnp

def _softmax(x, axis=-1):
    return jax.nn.softmax(x, axis=axis)

def _gelu(x):
    return jax.nn.gelu(x, approximate=True)

def _silu(x):
    return jax.nn.silu(x)

def _sigmoid(x):
    return jax.nn.sigmoid(x)

def _layernorm(x, axis=-1, eps=1e-05):
    m = jnp.mean(x, axis=axis, keepdims=True)
    v = jnp.var(x, axis=axis, keepdims=True)
    return (x - m) / jnp.sqrt(v + eps)

def _scatter_add(tgt, idx, src, axis=0):
    return tgt.at[idx].add(src)

def _segment_sum(src, seg, n):
    return jax.ops.segment_sum(src, seg, n)
kernel_name = 'mk_adj_resnorm_d1_adj_r2_86c158'

def setup_inputs(seed: int=0):
    np.random.seed(seed)
    _w = jnp.asarray

    def _rec_inputs():
        import jax
        import jax.numpy as jnp
        _gk = jax.random.key(seed)
        x = -0.0002928 + 1 * jax.random.normal(jax.random.fold_in(_gk, 1), (4096, 256), jnp.float32)
        _w = (1.0 + jnp.arange(4096, dtype=jnp.float32)) ** (-0.5)
        _w = _w / _w.mean()
        _pij = jnp.clip(0.00195312 * _w[:, None] * _w[None, :], 0.0, 1.0)
        _a = jax.random.uniform(jax.random.fold_in(_gk, 2), (4096, 4096)) < _pij
        adj = _a.astype(jnp.int32)
        return (x, adj)
    x, adj = _rec_inputs()

    def _L0_gnn_setup():
        import jax, jax.numpy as jnp
        import numpy as np
        N, D_IN, D_OUT = (4096, 256, 256)
        key = jax.random.key(seed)
        ks = jax.random.split(key, 8)
        scale_in = 1.0 / np.sqrt(D_IN)
        scale_cat = 1.0 / np.sqrt(2 * D_OUT)
        return {'x': jax.random.normal(ks[0], (N, D_IN), dtype=jnp.float32), 'adj': jax.random.randint(ks[1], (N, N), 0, 2, dtype=jnp.int32), 'W_self': jax.random.uniform(ks[2], (D_IN, D_OUT), jnp.float32, -scale_in, scale_in), 'b_self': jax.random.uniform(ks[3], (D_OUT,), jnp.float32, -scale_in, scale_in), 'W_nb': jax.random.uniform(ks[4], (D_IN, D_OUT), jnp.float32, -scale_in, scale_in), 'b_nb': jax.random.uniform(ks[5], (D_OUT,), jnp.float32, -scale_in, scale_in), 'W_comb': jax.random.uniform(ks[6], (2 * D_OUT, D_OUT), jnp.float32, -scale_cat, scale_cat), 'b_comb': jax.random.uniform(ks[7], (D_OUT,), jnp.float32, -scale_cat, scale_cat)}
    _L0_gnn_all = _L0_gnn_setup()
    _L0_gnn_in = {k: v for k, v in _L0_gnn_all.items() if k in ('W_self', 'b_self', 'W_nb', 'b_nb', 'W_comb', 'b_comb')}
    del _L0_gnn_all
    return {'x': x, 'adj': adj, 'L0_gnn_W_self': _L0_gnn_in['W_self'], 'L0_gnn_b_self': _L0_gnn_in['b_self'], 'L0_gnn_W_nb': _L0_gnn_in['W_nb'], 'L0_gnn_b_nb': _L0_gnn_in['b_nb'], 'L0_gnn_W_comb': _L0_gnn_in['W_comb'], 'L0_gnn_b_comb': _L0_gnn_in['b_comb']}

def reference(x, adj, L0_gnn_W_self, L0_gnn_b_self, L0_gnn_W_nb, L0_gnn_b_nb, L0_gnn_W_comb, L0_gnn_b_comb):
    import jax
    import jax.numpy as jnp

    def _L0_gnn_ref(x, adj, W_self, b_self, W_nb, b_nb, W_comb, b_comb):
        import jax, jax.numpy as jnp
        import numpy as np
        N, D_IN, D_OUT = (4096, 256, 256)
        mask = (adj > 0).astype(x.dtype)
        deg = jnp.sum(mask, axis=1, keepdims=True)
        agg = mask @ x / jnp.maximum(deg, 1.0)
        self_f = x @ W_self + b_self
        nb_f = agg @ W_nb + b_nb
        combined = jnp.concatenate([self_f, nb_f], axis=-1)
        out = combined @ W_comb + b_comb
        return jax.nn.relu(out)
    x = _layernorm(x + _L0_gnn_ref(x, adj, L0_gnn_W_self, L0_gnn_b_self, L0_gnn_W_nb, L0_gnn_b_nb, L0_gnn_W_comb, L0_gnn_b_comb), axis=-1)
    return x

_drawn_inputs = setup_inputs


def setup_inputs(seed=0):
    import zlib

    import numpy as np

    out = dict(_drawn_inputs(seed))
    spreads = {}
    factors = {'L0_gnn_b_self': 6.18, 'L0_gnn_b_nb': 5.235, 'L0_gnn_b_comb': 3.146}
    for name, (base, spread) in spreads.items():
        noise = np.random.default_rng([zlib.crc32(name.encode()), seed]).standard_normal(out[name].shape)
        drawn = base * np.exp(spread * noise) if base else spread * noise
        out[name] = jnp.asarray(drawn.astype(out[name].dtype))
    for name, factor in factors.items():
        out[name] = (out[name] * factor).astype(out[name].dtype)
    return out
```

```python
from contextlib import ExitStack

import concourse.bass as bass
from concourse import mybir

F32 = mybir.dt.float32
F16 = mybir.dt.float16
BF16 = mybir.dt.bfloat16
I32 = mybir.dt.int32
ALU = mybir.AluOpType
ACT = mybir.ActivationFunctionType
AX = mybir.AxisListType

P = 128
N = 4096
D = 256
KD = D // P
T = 4
GROUP = T * P
G = N // GROUP
Q = N // GROUP
NT = N // P
RING = 4
EPS = 1e-5
EXPONENT = 0x7F800000
TOP = 2.0 ** -14
LEAST = 2.0 ** -98



def gnn_layer(nc, adj_t, x_rows, x_t, w_nb, w_self, b_cols, b_comb, out):
    with ExitStack() as ctx:
        def sb(name, shape, dt):
            return ctx.enter_context(nc.sbuf_tensor(name, shape, dt))

        def psum(name):
            return ctx.enter_context(nc.psum_tensor(name, [P, 512], F32))

        def sem(name):
            return ctx.enter_context(nc.semaphore(name))

        adj_sb = sb("adj_sb", [P, RING, T, GROUP], I32)
        mask = sb("mask", [P, RING, T, GROUP], BF16)
        smask = sb("smask", [P, RING, T, GROUP], BF16)
        msum = sb("msum", [P, 2, T, GROUP], BF16)
        y = sb("y", [P, NT, 2 * D], F16)
        xt = sb("xt", [P, Q, KD * GROUP], F32)
        xt_cur = sb("xt_cur", [P, KD * GROUP], F32)
        x_sb = sb("x_sb", [P, 2, T, D], F32)
        wn_in = sb("wn_in", [P, 2 * KD, D], F32)
        ws_in = sb("ws_in", [P, 2 * KD, D], F32)
        b_in = sb("b_in", [P, 2 * KD], F32)
        b_wide = sb("b_wide", [P, 2 * KD, P], F32)
        bc = sb("bc", [P, D], F32)
        bias = sb("bias", [P, D], F32)
        wn = sb("wn", [P, KD, D], F32)
        ws = sb("ws", [P, KD, D], F32)
        ones = sb("ones", [P, P], F32)
        one = sb("one", [P, 2], BF16)
        eps = sb("eps", [P, 1], F32)
        rowmax = sb("rowmax", [P, NT], F32)
        power = sb("power", [P, NT], F32)
        scale = sb("scale", [P, NT], F32)
        unscale = sb("unscale", [P, NT], F32)
        z_sb = sb("z_sb", [P, T, D], F32)
        zb = sb("zb", [P, T, D], F32)
        deg1 = sb("deg1", [P, T], F32)
        rdeg = sb("rdeg", [P, T], F32)
        half = sb("half", [P, T, D], F32)
        pre = sb("pre", [P, T, D], F32)
        res = sb("res", [P, T, D], F32)
        stats = sb("stats", [P, T, 6], F32)
        mv = sb("mv", [P, T, 2], F32)
        std = sb("std", [P, T], F32)
        r0 = sb("r0", [P, T], F32)
        r_sq = sb("r_sq", [P, T], F32)
        r_err = sb("r_err", [P, T], F32)
        r_fix = sb("r_fix", [P, T], F32)
        rstd = sb("rstd", [P, T], F32)
        o_sb = sb("o_sb", [P, 2, T, D], F32)

        acc = [psum(f"acc{t}") for t in range(T)]
        yz = [psum(f"yz{b}") for b in range(3)]
        deg_ps = psum("deg_ps")

        adj_landed = [sem(f"adj_landed{s}") for s in range(RING)]
        xt_landed = [sem(f"xt_landed{q}") for q in range(Q)]
        x_landed = [sem(f"x_landed{s}") for s in range(2)]
        wn_landed = sem("wn_landed")
        ws_landed = sem("ws_landed")
        b_landed = sem("b_landed")
        bc_landed = sem("bc_landed")
        out_stored = [sem(f"out_stored{s}") for s in range(2)]
        ones_set = sem("ones_set")
        consts_set = sem("consts_set")
        b_widened = sem("b_widened")
        wn_product = sem("wn_product")
        ws_product = sem("ws_product")
        b_product = sem("b_product")
        wn_ready = sem("wn_ready")
        ws_ready = sem("ws_ready")
        bias_ready = sem("bias_ready")
        y_product = sem("y_product")
        rowmax_ready = sem("rowmax_ready")
        power_ready = sem("power_ready")
        scale_ready = sem("scale_ready")
        unscale_ready = sem("unscale_ready")
        hi_ready = sem("hi_ready")
        lo_ready = sem("lo_ready")
        mask_ready = sem("mask_ready")
        smask_ready = sem("smask_ready")
        quad_done = sem("quad_done")
        acc_done = sem("acc_done")
        msum_ready = sem("msum_ready")
        deg_done = sem("deg_done")
        xt_cur_ready = sem("xt_cur_ready")
        z_done = sem("z_done")
        z_copied = sem("z_copied")
        zb_ready = sem("zb_ready")
        deg1_ready = sem("deg1_ready")
        rdeg_ready = sem("rdeg_ready")
        half_ready = sem("half_ready")
        pre_ready = sem("pre_ready")
        res_ready = sem("res_ready")
        stats_ready = sem("stats_ready")
        var_ready = sem("var_ready")
        std_ready = sem("std_ready")
        r0_ready = sem("r0_ready")
        r_sq_ready = sem("r_sq_ready")
        r_err_ready = sem("r_err_ready")
        r_fix_ready = sem("r_fix_ready")
        rstd_ready = sem("rstd_ready")
        o_ready = sem("o_ready")

        def y_ps(i):
            return yz[(i // 2) % 3][:, (i % 2) * D:(i % 2 + 1) * D]

        def z_ps(t):
            return yz[1 + t % 2][:, 0:D]

        block = ctx.enter_context(nc.Block())

        @block.sync
        def _(sp):
            def load_adj(g, q):
                if not (isinstance(g, int) and g == 0 and q < RING):
                    sp.wait_ge(mask_ready, Q * g + q + 1 - RING)
                sp.dma_start(adj_sb[:, q % RING, :, :], adj_t[g, q]).then_inc(adj_landed[q % RING], 16)

            def load_x(g, slot):
                if not (isinstance(g, int) and g < 2):
                    sp.wait_ge(res_ready, T * (g - 1))
                sp.dma_start(x_sb[:, slot, :, :], x_rows[g]).then_inc(x_landed[slot], 16)

            def store(g, slot):
                sp.wait_ge(o_ready, T * (g + 1))
                sp.dma_start(out[g], o_sb[:, slot, :, :]).then_inc(out_stored[slot], 16)

            def load_xt(q):
                sp.dma_start(xt[:, q, :], x_t[q]).then_inc(xt_landed[q], 16)

            sp.dma_start(wn_in[:], w_nb).then_inc(wn_landed, 16)
            load_xt(0)
            load_adj(0, 0)
            sp.dma_start(b_in[:], b_cols).then_inc(b_landed, 16)
            sp.dma_start(bc[:], b_comb).then_inc(bc_landed, 16)
            load_xt(1)
            load_adj(0, 1)
            sp.dma_start(ws_in[:], w_self).then_inc(ws_landed, 16)
            load_xt(2)
            load_xt(3)
            load_adj(0, 2)
            load_xt(4)
            load_xt(5)
            load_adj(0, 3)
            load_xt(6)
            load_xt(7)
            load_x(0, 0)
            for q in range(4, Q):
                load_adj(0, q)
            for q in range(Q):
                load_adj(1, q)
            load_x(1, 1)

            with sp.Fori(1, G // 2) as pair:
                for odd in range(2):
                    g = 2 * pair + odd
                    for q in range(Q):
                        load_adj(g, q)
                        if q == 3:
                            store(g - 2, odd)
                        if q == 4:
                            load_x(g, odd)
            store(G - 2, 0)
            sp.wait_ge(out_stored[0], 16 * G // 2)
            for t in range(T):
                sp.wait_ge(o_ready, T * (G - 1) + t + 1)
                sp.dma_start(out[G - 1, :, t, :], o_sb[:, 1, t, :]).then_inc(out_stored[1], 16)
            sp.wait_ge(out_stored[1], 16 * (G // 2 - 1 + T))

        @block.gpsimd
        def _(pool):
            def group(g):
                if not (isinstance(g, int) and g == 0):
                    pool.wait_ge(z_done, T * g)
                    nc.gpsimd.tensor_copy(xt_cur[:, :], xt[:, bass.ds(g, 1), :].rearrange("p a n -> p (a n)")).then_inc(xt_cur_ready, 1)
                for t in range(T):
                    pool.wait_ge(z_copied, T * g + t + 1)
                    if not (isinstance(g, int) and g == 0):
                        pool.wait_ge(pre_ready, T * (g - 1) + t + 1)
                    nc.gpsimd.tensor_tensor(zb[:, t, :], z_sb[:, t, :], bias[:], ALU.add).then_inc(zb_ready, 1)

            for q in range(Q):
                pool.wait_ge(xt_landed[q], 16)
            pool.wait_ge(bias_ready, 1)
            group(0)
            group(1)
            with pool.Fori(1, G // 2) as pair:
                for odd in range(2):
                    group(2 * pair + odd)

        @block.scalar
        def _(act):
            def scale_mask(g, q, tiles):
                act.wait_ge(mask_ready, Q * g + q + 1)
                if not (isinstance(g, int) and g == 0 and q < RING):
                    act.wait_ge(quad_done, Q * g + q + 1 - RING)
                for j in tiles:
                    last = nc.scalar.activation(smask[:, q % RING, j, :], mask[:, q % RING, j, :], ACT.Copy,
                                                scale=scale[:, T * q + j:T * q + j + 1])
                if j == T - 1:
                    last.then_inc(smask_ready, 1)

            def copy_z(g, t):
                act.wait_ge(z_done, T * g + t + 1)
                if not (isinstance(g, int) and g == 0):
                    act.wait_ge(zb_ready, T * (g - 1) + t + 1)
                nc.scalar.activation(z_sb[:, t, :], z_ps(t), ACT.Copy).then_inc(z_copied, 1)

            def std_of(g):
                act.wait_ge(var_ready, T * (g + 1))
                nc.scalar.activation(std[:], mv[:, :, 1], ACT.Sqrt, bias=eps[:]).then_inc(std_ready, 1)

            def group(g):
                for q in range(Q):
                    scale_mask(g, q, range(T))
                    if 3 <= q < 3 + T:
                        copy_z(g, q - 3)
                    if q == 5:
                        std_of(g - 1)

            act.wait_ge(consts_set, 2)
            act.wait_ge(wn_product, 1)
            nc.scalar.activation(wn[:], acc[0][:].rearrange("p (k n) -> p k n", k=KD), ACT.Copy).then_inc(wn_ready, 1)
            for m in range(NT // 2):
                act.wait_ge(unscale_ready, m + 1)
                for i in (2 * m, 2 * m + 1):
                    nc.scalar.activation(y[:, i, 0:D], y_ps(i), ACT.Copy,
                                         scale=unscale[:, i:i + 1]).then_inc(hi_ready, 1)
                scale_mask(0, m // 2, range(2 * (m % 2), 2 * (m % 2) + 2))
                if m == 0:
                    act.wait_ge(ws_product, 1)
                    nc.scalar.activation(ws[:], acc[1][:].rearrange("p (k n) -> p k n", k=KD), ACT.Copy).then_inc(ws_ready, 1)
            for t in range(T):
                copy_z(0, t)
            group(1)
            with act.Fori(1, G // 2) as pair:
                for odd in range(2):
                    group(2 * pair + odd)
            std_of(G - 1)

        @block.vector
        def _(dve):
            def to_mask(g, q):
                dve.wait_ge(adj_landed[q % RING], 16 * ((Q // RING) * g + q // RING + 1))
                if not (isinstance(g, int) and g == 0 and q < RING):
                    dve.wait_ge(smask_ready, Q * g + q + 1 - RING)
                nc.vector.tensor_scalar(mask[:, q % RING, :, :], adj_sb[:, q % RING, :, :], 0.0, None,
                                        ALU.is_gt).then_inc(mask_ready, 1)

            def sum_masks(g, q, odd):
                dve.wait_ge(mask_ready, Q * g + q + 1)
                if q == 1:
                    if not (isinstance(g, int) and g < 2):
                        dve.wait_ge(deg_done, g - 1)
                    first = mask[:, 0, :, :]
                else:
                    dve.wait_ge(msum_ready, (Q - 1) * g + q - 1)
                    first = msum[:, odd, :, :]
                nc.vector.tensor_tensor(msum[:, odd, :, :], first, mask[:, q % RING, :, :],
                                        ALU.add).then_inc(msum_ready, 1)

            def invert_deg(g):
                dve.wait_ge(deg_done, g + 1)
                nc.vector.tensor_scalar(deg1[:], deg_ps[:, 0:T], 1.0, None, ALU.max).then_inc(deg1_ready, 1)
                dve.wait_ge(deg1_ready, g + 1)
                nc.vector.reciprocal(rdeg[:], deg1[:]).then_inc(rdeg_ready, 1)

            def drain_acc(g, t):
                dve.wait_ge(rdeg_ready, g + 1)
                dve.wait_ge(zb_ready, T * g + t + 1)
                if t < T - 1:
                    dve.wait_ge(acc_done, (T - 1) * g + t + 1)
                else:
                    dve.wait_ge(quad_done, Q * (g + 1))
                nc.vector.scalar_tensor_tensor(out=half[:, t, :], in0=acc[t][:, 0:D], scalar=rdeg[:, t:t + 1],
                                               in1=zb[:, t, :], op0=ALU.mult, op1=ALU.add).then_inc(half_ready, 1)
                dve.wait_ge(half_ready, T * g + t + 1)
                nc.vector.scalar_tensor_tensor(out=pre[:, t, :], in0=acc[t][:, D:2 * D], scalar=rdeg[:, t:t + 1],
                                               in1=half[:, t, :], op0=ALU.mult, op1=ALU.add).then_inc(pre_ready, 1)

            def add_x(g, t, odd):
                if t == 0:
                    dve.wait_ge(x_landed[odd], 16 * ((g - odd) // 2 + 1) if isinstance(g, int) else 8 * (g - odd) + 16)
                dve.wait_ge(pre_ready, T * g + t + 1)
                nc.vector.scalar_tensor_tensor(out=res[:, t, :], in0=pre[:, t, :], scalar=0.0,
                                               in1=x_sb[:, odd, t, :], op0=ALU.max, op1=ALU.add).then_inc(res_ready, 1)

            def row_stats(g, t):
                dve.wait_ge(res_ready, T * g + t + 1)
                nc.vector.bn_stats(stats[:, t, :], res[:, t, :]).then_inc(stats_ready, 1)

            def row_var(t):
                nc.vector.bn_aggr(mv[:, t, :], stats[:, t, :]).then_inc(var_ready, 1)

            def invert_std(g):
                dve.wait_ge(std_ready, g + 1)
                nc.vector.reciprocal(r0[:], std[:]).then_inc(r0_ready, 1)
                dve.wait_ge(r0_ready, g + 1)
                nc.vector.tensor_tensor(r_sq[:], r0[:], r0[:], ALU.mult).then_inc(r_sq_ready, 1)
                dve.wait_ge(r_sq_ready, g + 1)
                nc.vector.scalar_tensor_tensor(out=r_err[:], in0=mv[:, :, 1], scalar=EPS, in1=r_sq[:],
                                               op0=ALU.add, op1=ALU.mult).then_inc(r_err_ready, 1)
                dve.wait_ge(r_err_ready, g + 1)
                nc.vector.tensor_scalar(r_fix[:], r_err[:], -0.5, 1.5, ALU.mult, ALU.add).then_inc(r_fix_ready, 1)
                dve.wait_ge(r_fix_ready, g + 1)
                nc.vector.tensor_tensor(rstd[:], r0[:], r_fix[:], ALU.mult).then_inc(rstd_ready, 1)

            def normalise(g, t, odd):
                if t == 0:
                    dve.wait_ge(rstd_ready, g + 1)
                    if not (isinstance(g, int) and g < 2):
                        dve.wait_ge(out_stored[odd], 16 * ((g - odd) // 2) if isinstance(g, int) else 8 * (g - odd))
                nc.vector.tensor_scalar(o_sb[:, odd, t, :], res[:, t, :], mv[:, t, 0:1], rstd[:, t:t + 1],
                                        ALU.subtract, ALU.mult).then_inc(o_ready, 1)

            def group(g, odd):
                h, h_odd = g - 1, 1 - odd
                for q in range(Q):
                    to_mask(g, q)
                    if q == 5:
                        dve.wait_ge(stats_ready, T * (h + 1))
                    if q > 1:
                        sum_masks(g, q - 1, odd)
                    if q == 2:
                        invert_deg(h)
                    if q == 3:
                        for t in range(T):
                            drain_acc(h, t)
                        for t in range(2):
                            add_x(h, t, h_odd)
                    if q == 4:
                        for t in range(2, T):
                            add_x(h, t, h_odd)
                        for t in range(T):
                            row_stats(h, t)
                    if q == 5:
                        for t in range(T):
                            row_var(t)
                    if q == 7:
                        sum_masks(g, q, odd)
                        invert_std(h)
                        for t in range(T):
                            normalise(h, t, h_odd)

            nc.vector.memset(ones[:], 1.0).then_inc(ones_set, 1)
            nc.vector.memset(one[:], 1.0).then_inc(consts_set, 1)
            nc.vector.memset(eps[:], EPS).then_inc(consts_set, 1)
            dve.wait_ge(b_landed, 16)
            dve.wait_ge(ones_set, 1)
            for k in range(2 * KD):
                nc.vector.tensor_scalar(b_wide[:, k, :], ones[:], b_in[:, k:k + 1], None, ALU.mult).then_inc(b_widened, 1)

            def split_lo(i):
                dve.wait_ge(hi_ready, i + 2 - i % 2)
                nc.vector.scalar_tensor_tensor(out=y[:, i, D:2 * D], in0=y_ps(i), scalar=unscale[:, i:i + 1],
                                               in1=y[:, i, 0:D], op0=ALU.mult, op1=ALU.subtract).then_inc(lo_ready, 1)

            for m in range(NT // 2):
                two = slice(2 * m, 2 * m + 2)
                if m % 2 == 0:
                    to_mask(0, m // 2)
                dve.wait_ge(y_product, m + 1)
                nc.vector.tensor_reduce(rowmax[:, two], yz[m % 3][:].rearrange("p (a n) -> p a n", a=2), AX.X,
                                        ALU.max, apply_absolute_value=True).then_inc(rowmax_ready, 1)
                if m:
                    split_lo(2 * m - 2)
                dve.wait_ge(rowmax_ready, m + 1)
                nc.vector.tensor_scalar(power[:, two].bitcast(I32), rowmax[:, two].bitcast(I32), EXPONENT, None,
                                        ALU.bitwise_and).then_inc(power_ready, 1)
                if m:
                    split_lo(2 * m - 1)
                dve.wait_ge(power_ready, m + 1)
                nc.vector.tensor_scalar(scale[:, two], power[:, two], LEAST, TOP, ALU.max,
                                        ALU.mult).then_inc(scale_ready, 1)
                dve.wait_ge(scale_ready, m + 1)
                nc.vector.reciprocal(unscale[:, two], scale[:, two]).then_inc(unscale_ready, 1)
                if m % 2 and m // 2:
                    sum_masks(0, m // 2, 0)
                if m == 1:
                    dve.wait_ge(b_product, 1)
                    dve.wait_ge(bc_landed, 16)
                    nc.vector.tensor_tensor(bias[:], acc[2][:, 0:D], bc[:], ALU.add).then_inc(bias_ready, 1)
            split_lo(NT - 2)
            split_lo(NT - 1)

            group(1, 1)
            with dve.Fori(1, G // 2) as pair:
                for odd in range(2):
                    group(2 * pair + odd, odd)
            h = G - 1
            invert_deg(h)
            for t in range(T):
                drain_acc(h, t)
                add_x(h, t, 1)
                row_stats(h, t)
                dve.wait_ge(stats_ready, T * h + t + 1)
                row_var(t)
            invert_std(h)
            for t in range(T):
                normalise(h, t, 1)

        @block.tensor
        def _(pe):
            def fold(dst, w, done):
                for a in range(KD):
                    for k in range(KD):
                        last = nc.tensor.matmul(dst[:, a * D:(a + 1) * D], w[:, k, a * P:(a + 1) * P], w[:, KD + k, :],
                                                start=(k == 0), stop=(k == KD - 1))
                last.then_inc(done, 1)

            def quad_products(g, q, tiles):
                pe.wait_ge(smask_ready, Q * g + q + 1)
                for t in tiles:
                    if q == 0 and not (isinstance(g, int) and g == 0):
                        pe.wait_ge(pre_ready, T * (g - 1) + t + 1)
                    for j in range(T):
                        last = nc.tensor.matmul(acc[t][:], smask[:, q % RING, j, t * P:(t + 1) * P],
                                                y[:, T * q + j, :], start=(q == 0 and j == 0),
                                                stop=(q == Q - 1 and j == T - 1))
                    if t == T - 1:
                        last.then_inc(quad_done, 1)
                    elif q == Q - 1:
                        last.then_inc(acc_done, 1)

            def degrees(g, odd):
                pe.wait_ge(msum_ready, (Q - 1) * (g + 1))
                if not (isinstance(g, int) and g == 0):
                    pe.wait_ge(deg1_ready, g)
                for t in range(T):
                    for j in range(T):
                        last = nc.tensor.matmul(deg_ps[:, t:t + 1], msum[:, odd, j, t * P:(t + 1) * P], one[:, 0:1],
                                                start=(j == 0), stop=(j == T - 1))
                last.then_inc(deg_done, 1)

            def z_product(g, t, src):
                for k in range(KD):
                    last = nc.tensor.matmul(z_ps(t), src[:, k * GROUP + t * P:k * GROUP + (t + 1) * P], ws[:, k, :],
                                            start=(k == 0), stop=(k == KD - 1))
                last.then_inc(z_done, 1)

            def group(g, odd):
                for q in range(Q):
                    if q == Q - 1:
                        degrees(g, odd)
                    quad_products(g, q, range(T))
                    if q < T:
                        if q == 0:
                            pe.wait_ge(xt_cur_ready, g)
                        pe.wait_ge(z_copied, T * g + q - 1)
                        z_product(g, q, xt_cur)

            pe.wait_ge(wn_landed, 16)
            fold(acc[0], wn_in, wn_product)

            y_ahead = 3
            for m in range(NT // 2 + y_ahead):
                if m < NT // 2:
                    if m == 0:
                        pe.wait_ge(wn_ready, 1)
                    if m % 2 == 0:
                        pe.wait_ge(xt_landed[m // 2], 16)
                    if m >= 3:
                        pe.wait_ge(lo_ready, 2 * m - 4)
                    for i in (2 * m, 2 * m + 1):
                        for k in range(KD):
                            at = k * GROUP + (i % T) * P
                            last = nc.tensor.matmul(y_ps(i), xt[:, i // T, at:at + P], wn[:, k, :],
                                                    start=(k == 0), stop=(k == KD - 1))
                    last.then_inc(y_product, 1)
                elif m < NT // 2 + 2:
                    if m == NT // 2:
                        pe.wait_ge(ws_ready, 1)
                    for t in (2 * (m - NT // 2), 2 * (m - NT // 2) + 1):
                        if t < 2:
                            pe.wait_ge(lo_ready, NT - T + 2 * t)
                        else:
                            pe.wait_ge(z_copied, t - 1)
                        z_product(0, t, xt[:, 0, :])
                if m == 0:
                    pe.wait_ge(ws_landed, 16)
                    fold(acc[1], ws_in, ws_product)
                    pe.wait_ge(b_widened, 2 * KD)
                    for k in range(2 * KD):
                        w = ws_in if k < KD else wn_in
                        last = nc.tensor.matmul(acc[2][:, 0:D], b_wide[:, k, :], w[:, KD + k % KD, :],
                                                start=(k == 0), stop=(k == 2 * KD - 1))
                    last.then_inc(b_product, 1)
                if m >= y_ahead:
                    unit = m - y_ahead
                    if unit == 0:
                        pe.wait_ge(bias_ready, 1)
                        pe.wait_ge(ws_ready, 1)
                    if unit % 2 == 0:
                        pe.wait_ge(lo_ready, 2 * unit + T)
                    if unit == 2 * (Q - 1):
                        degrees(0, 0)
                    quad_products(0, unit // 2, (0, 1) if unit % 2 == 0 else (2, 3))

            group(1, 1)
            with pe.Fori(1, G // 2) as pair:
                for odd in range(2):
                    group(2 * pair + odd, odd)


def kernel(x, adj, L0_gnn_W_self, L0_gnn_b_self, L0_gnn_W_nb, L0_gnn_b_nb, L0_gnn_W_comb, L0_gnn_b_comb):
    import numpy as np
    import concourse.bacc as bacc
    from concourse.bass_utils import run_bass_kernel_spmd

    def rows(w):
        w = np.asarray(w)
        return w.reshape(KD, P, -1).transpose(1, 0, 2)

    x, adj = np.asarray(x), np.asarray(adj)
    wc = np.asarray(L0_gnn_W_comb)
    ins = {
        "adj_t": np.ascontiguousarray(adj.reshape(G, P, T, Q, P, T).transpose(0, 3, 4, 5, 2, 1).reshape(G, Q, P, T, GROUP)),
        "x_rows": np.ascontiguousarray(x.reshape(G, P, T, D)),
        "x_t": np.ascontiguousarray(x.reshape(Q, P, T, KD, P).transpose(0, 4, 3, 2, 1).reshape(Q, P, KD * GROUP)),
        "w_nb": np.ascontiguousarray(np.concatenate([rows(np.asarray(L0_gnn_W_nb).T), rows(wc[D:])], axis=1)),
        "w_self": np.ascontiguousarray(np.concatenate([rows(np.asarray(L0_gnn_W_self).T), rows(wc[:D])], axis=1)),
        "b_cols": np.ascontiguousarray(np.concatenate([np.asarray(L0_gnn_b_self).reshape(KD, P), np.asarray(L0_gnn_b_nb).reshape(KD, P)]).T),
        "b_comb": np.ascontiguousarray(np.broadcast_to(np.asarray(L0_gnn_b_comb), (P, D))),
    }
    nc = bacc.Bacc("TRN2", target_bir_lowering=False, num_devices=1)
    aps = {name: nc.dram_tensor(name, a.shape, mybir.dt.from_np(a.dtype), kind="ExternalInput").ap()
           for name, a in ins.items()}
    out = nc.dram_tensor("out", (G, P, T, D), F32, kind="ExternalOutput").ap()
    gnn_layer(nc, out=out, **aps)
    r = run_bass_kernel_spmd(nc, [ins], core_ids=[0])
    return r.results[0]["out"].reshape(N, D)
```

```python
from contextlib import ExitStack

import concourse.bass as bass
from concourse import mybir

F32 = mybir.dt.float32
F16 = mybir.dt.float16
BF16 = mybir.dt.bfloat16
I32 = mybir.dt.int32
ALU = mybir.AluOpType
ACT = mybir.ActivationFunctionType
AX = mybir.AxisListType

P = 128
N = 4096
D = 256
KD = D // P
T = 4
GROUP = T * P
G = N // GROUP
Q = N // GROUP
NT = N // P
RING = 4
WARM = 8
EPS = 1e-5
EXPONENT = 0x7F800000
TOP = 2.0 ** -14
LEAST = 2.0 ** -98



def gnn_layer(nc, adj_t, x_rows, x_t, w_nb, w_self, b_cols, b_comb, out):
    with ExitStack() as ctx:
        def sb(name, shape, dt):
            return ctx.enter_context(nc.sbuf_tensor(name, shape, dt))

        def psum(name):
            return ctx.enter_context(nc.psum_tensor(name, [P, 512], F32))

        def sem(name):
            return ctx.enter_context(nc.semaphore(name))

        adj_sb = sb("adj_sb", [P, RING, T, GROUP], I32)
        mask = sb("mask", [P, RING, T, GROUP], BF16)
        smask = sb("smask", [P, RING, T, GROUP], BF16)
        msum = sb("msum", [P, T, GROUP], BF16)
        y = sb("y", [P, NT, 2 * D], F16)
        xt = sb("xt", [P, Q, KD * GROUP], F32)
        xt_cur = sb("xt_cur", [P, KD * GROUP], F32)
        x_sb = sb("x_sb", [P, T, D], F32)
        wn_in = sb("wn_in", [P, 2 * KD, D], F32)
        ws_in = sb("ws_in", [P, 2 * KD, D], F32)
        b_in = sb("b_in", [P, 2 * KD], F32)
        b_wide = sb("b_wide", [P, 2 * KD, P], F32)
        bc = sb("bc", [P, D], F32)
        bias = sb("bias", [P, D], F32)
        wn = sb("wn", [P, KD, D], F32)
        ws = sb("ws", [P, KD, D], F32)
        ones = sb("ones", [P, P], F32)
        one = sb("one", [P, 2], BF16)
        eps = sb("eps", [P, 1], F32)
        rowmax = sb("rowmax", [P, NT], F32)
        power = sb("power", [P, NT], F32)
        scale = sb("scale", [P, NT], F32)
        unscale = sb("unscale", [P, NT], F32)
        z_sb = sb("z_sb", [P, T, D], F32)
        zb = sb("zb", [P, T, D], F32)
        deg1 = sb("deg1", [P, T], F32)
        rdeg = sb("rdeg", [P, T], F32)
        half = sb("half", [P, T, D], F32)
        pre = sb("pre", [P, T, D], F32)
        res = sb("res", [P, T, D], F32)
        stats = sb("stats", [P, T, 6], F32)
        mv = sb("mv", [P, T, 2], F32)
        std = sb("std", [P, T], F32)
        r0 = sb("r0", [P, T], F32)
        r_sq = sb("r_sq", [P, T], F32)
        r_err = sb("r_err", [P, T], F32)
        r_fix = sb("r_fix", [P, T], F32)
        rstd = sb("rstd", [P, T], F32)
        x_last = sb("x_last", [P, T, D], F32)
        o_sb = sb("o_sb", [P, T, D], F32)
        warm = sb("warm", [P, 512], BF16)

        acc = [psum(f"acc{t}") for t in range(T)]
        yz = [psum(f"yz{b}") for b in range(3)]
        deg_ps = psum("deg_ps")

        adj_landed = [sem(f"adj_landed{s}") for s in range(RING)]
        xt_landed = [sem(f"xt_landed{q}") for q in range(Q)]
        x_landed = sem("x_landed")
        x_last_landed = sem("x_last_landed")
        wn_landed = sem("wn_landed")
        ws_landed = sem("ws_landed")
        b_landed = sem("b_landed")
        bc_landed = sem("bc_landed")
        out_stored = sem("out_stored")
        last_stored = sem("last_stored")
        warm_set = sem("warm_set")
        ones_set = sem("ones_set")
        consts_set = sem("consts_set")
        b_widened = sem("b_widened")
        wn_product = sem("wn_product")
        ws_product = sem("ws_product")
        b_product = sem("b_product")
        wn_ready = sem("wn_ready")
        ws_ready = sem("ws_ready")
        bias_ready = sem("bias_ready")
        y_product = sem("y_product")
        rowmax_ready = sem("rowmax_ready")
        power_ready = sem("power_ready")
        scale_ready = sem("scale_ready")
        unscale_ready = sem("unscale_ready")
        hi_ready = sem("hi_ready")
        lo_ready = sem("lo_ready")
        mask_ready = sem("mask_ready")
        smask_ready = sem("smask_ready")
        quad_done = sem("quad_done")
        acc_done = sem("acc_done")
        msum_ready = sem("msum_ready")
        deg_done = sem("deg_done")
        xt_cur_ready = sem("xt_cur_ready")
        z_done = sem("z_done")
        z_copied = sem("z_copied")
        zb_ready = sem("zb_ready")
        deg1_ready = sem("deg1_ready")
        rdeg_ready = sem("rdeg_ready")
        half_ready = sem("half_ready")
        pre_ready = sem("pre_ready")
        res_ready = sem("res_ready")
        stats_ready = sem("stats_ready")
        var_ready = sem("var_ready")
        std_ready = sem("std_ready")
        r0_ready = sem("r0_ready")
        r_sq_ready = sem("r_sq_ready")
        r_err_ready = sem("r_err_ready")
        r_fix_ready = sem("r_fix_ready")
        rstd_ready = sem("rstd_ready")
        o_ready = sem("o_ready")

        def y_ps(i):
            return yz[(i // 2) % 3][:, (i % 2) * D:(i % 2 + 1) * D]

        def z_ps(t):
            return yz[1 + t % 2][:, 0:D]

        block = ctx.enter_context(nc.Block())

        @block.sync
        def _(sp):
            def load_adj(g, q):
                if not (isinstance(g, int) and g == 0 and q < RING):
                    sp.wait_ge(mask_ready, Q * g + q + 1 - RING)
                sp.dma_start(adj_sb[:, q % RING, :, :], adj_t[g, q]).then_inc(adj_landed[q % RING], 16)

            def load_xt(q):
                sp.dma_start(xt[:, q, :], x_t[q]).then_inc(xt_landed[q], 16)

            sp.dma_start(wn_in[:], w_nb).then_inc(wn_landed, 16)
            sp.dma_start(ws_in[:], w_self).then_inc(ws_landed, 16)
            load_xt(0)
            load_adj(0, 0)
            sp.dma_start(b_in[:], b_cols).then_inc(b_landed, 16)
            sp.dma_start(bc[:], b_comb).then_inc(bc_landed, 16)
            load_xt(1)
            load_adj(0, 1)
            load_xt(2)
            load_xt(3)
            load_adj(0, 2)
            load_xt(4)
            load_xt(5)
            load_adj(0, 3)
            load_xt(6)
            load_xt(7)
            for q in range(4, Q):
                load_adj(0, q)
            sp.dma_start(x_last[:], x_rows[G - 1]).then_inc(x_last_landed, 16)
            with sp.Fori(1, G) as g:
                for q in range(Q):
                    load_adj(g, q)
            for t in range(T):
                sp.wait_ge(o_ready, T * (G - 1) + t + 1)
                sp.dma_start(out[G - 1, :, t, :], o_sb[:, t, :]).then_inc(last_stored, 16)
            sp.wait_ge(last_stored, 16 * T)

        @block.gpsimd
        def _(pool):
            def add_bias(g):
                for t in range(T):
                    pool.wait_ge(z_copied, T * g + t + 1)
                    if not (isinstance(g, int) and g == 0):
                        pool.wait_ge(pre_ready, T * (g - 1) + t + 1)
                    nc.gpsimd.tensor_tensor(zb[:, t, :], z_sb[:, t, :], bias[:], ALU.add).then_inc(zb_ready, 1)

            for q in range(Q):
                pool.wait_ge(xt_landed[q], 16)
            pool.dma_start(x_sb[:], x_rows[0]).then_inc(x_landed, 16)
            pool.wait_ge(bias_ready, 1)
            add_bias(0)
            def group(g):
                pool.wait_ge(z_done, T * g)
                nc.gpsimd.tensor_copy(xt_cur[:, :], xt[:, bass.ds(g, 1), :].rearrange("p a n -> p (a n)")).then_inc(xt_cur_ready, 1)
                add_bias(g)
                pool.wait_ge(o_ready, T * g)
                pool.dma_start(out[bass.ds(g - 1, 1)].rearrange("a p t n -> p (a t) n"), o_sb[:]).then_inc(out_stored, 16)

            with pool.Fori(1, G - 1) as g:
                group(g)
                pool.wait_ge(out_stored, 16 * g)
                pool.dma_start(x_sb[:], x_rows[bass.ds(g, 1)].rearrange("a p t n -> p (a t) n")).then_inc(x_landed, 16)
            group(G - 1)
            pool.wait_ge(out_stored, 16 * (G - 1))

        @block.scalar
        def _(act):
            def scale_mask(g, q, tiles):
                act.wait_ge(mask_ready, Q * g + q + 1)
                if not (isinstance(g, int) and g == 0 and q < RING):
                    act.wait_ge(quad_done, Q * g + q + 1 - RING)
                for j in tiles:
                    last = nc.scalar.activation(smask[:, q % RING, j, :], mask[:, q % RING, j, :], ACT.Copy,
                                                scale=scale[:, T * q + j:T * q + j + 1])
                if j == T - 1:
                    last.then_inc(smask_ready, 1)

            def copy_z(g, t):
                act.wait_ge(z_done, T * g + t + 1)
                if not (isinstance(g, int) and g == 0):
                    act.wait_ge(zb_ready, T * (g - 1) + t + 1)
                nc.scalar.activation(z_sb[:, t, :], z_ps(t), ACT.Copy).then_inc(z_copied, 1)

            def std_of(g, first, end):
                act.wait_ge(var_ready, T * g + end)
                nc.scalar.activation(std[:, first:end], mv[:, first:end, 1], ACT.Sqrt, bias=eps[:]).then_inc(std_ready, 1)

            def group(g):
                for q in range(Q):
                    scale_mask(g, q, range(T))
                    if 3 <= q < 3 + T:
                        copy_z(g, q - 3)
                    if q == 5:
                        std_of(g - 1, 0, T)

            act.wait_ge(consts_set, 2)
            nc.scalar.activation(std[:, 0:1], eps[:], ACT.Sqrt)
            act.wait_ge(wn_product, 1)
            nc.scalar.activation(wn[:], acc[0][:].rearrange("p (k n) -> p k n", k=KD), ACT.Copy).then_inc(wn_ready, 1)
            act.wait_ge(ws_product, 1)
            nc.scalar.activation(ws[:], acc[1][:].rearrange("p (k n) -> p k n", k=KD), ACT.Copy).then_inc(ws_ready, 1)
            for m in range(NT // 2):
                act.wait_ge(unscale_ready, m + 1)
                for i in (2 * m, 2 * m + 1):
                    nc.scalar.activation(y[:, i, 0:D], y_ps(i), ACT.Copy,
                                         scale=unscale[:, i:i + 1]).then_inc(hi_ready, 1)
                scale_mask(0, m // 2, range(2 * (m % 2), 2 * (m % 2) + 2))
            for t in range(T):
                copy_z(0, t)
            with act.Fori(1, G) as g:
                group(g)
            for t in range(T):
                std_of(G - 1, t, t + 1)

        @block.vector
        def _(dve):
            def to_mask(g, q):
                dve.wait_ge(adj_landed[q % RING], 16 * ((Q // RING) * g + q // RING + 1))
                if not (isinstance(g, int) and g == 0 and q < RING):
                    dve.wait_ge(smask_ready, Q * g + q + 1 - RING)
                nc.vector.tensor_scalar(mask[:, q % RING, :, :], adj_sb[:, q % RING, :, :], 0.0, None,
                                        ALU.is_gt).then_inc(mask_ready, 1)

            def sum_masks(g, q):
                dve.wait_ge(mask_ready, Q * g + q + 1)
                if q == 1:
                    if not (isinstance(g, int) and g == 0):
                        dve.wait_ge(deg_done, g)
                    first = mask[:, 0, :, :]
                else:
                    dve.wait_ge(msum_ready, (Q - 1) * g + q - 1)
                    first = msum[:, :, :]
                nc.vector.tensor_tensor(msum[:, :, :], first, mask[:, q % RING, :, :],
                                        ALU.add).then_inc(msum_ready, 1)

            def invert_deg(g):
                dve.wait_ge(deg_done, g + 1)
                nc.vector.tensor_scalar(deg1[:], deg_ps[:, 0:T], 1.0, None, ALU.max).then_inc(deg1_ready, 1)
                dve.wait_ge(deg1_ready, g + 1)
                nc.vector.reciprocal(rdeg[:], deg1[:]).then_inc(rdeg_ready, 1)

            def drain_acc(g, t, own_count):
                dve.wait_ge(rdeg_ready, g + 1)
                dve.wait_ge(zb_ready, T * g + t + 1)
                if own_count:
                    dve.wait_ge(acc_done, (T - 1) * g + t + 1)
                else:
                    dve.wait_ge(quad_done, Q * (g + 1))
                nc.vector.scalar_tensor_tensor(out=half[:, t, :], in0=acc[t][:, 0:D], scalar=rdeg[:, t:t + 1],
                                               in1=zb[:, t, :], op0=ALU.mult, op1=ALU.add).then_inc(half_ready, 1)
                dve.wait_ge(half_ready, T * g + t + 1)
                nc.vector.scalar_tensor_tensor(out=pre[:, t, :], in0=acc[t][:, D:2 * D], scalar=rdeg[:, t:t + 1],
                                               in1=half[:, t, :], op0=ALU.mult, op1=ALU.add).then_inc(pre_ready, 1)

            def add_x(g, t, x_in):
                if t == 0:
                    if x_in is x_last:
                        dve.wait_ge(x_last_landed, 16)
                    else:
                        dve.wait_ge(x_landed, 16 * (g + 1))
                dve.wait_ge(pre_ready, T * g + t + 1)
                nc.vector.scalar_tensor_tensor(out=res[:, t, :], in0=pre[:, t, :], scalar=0.0,
                                               in1=x_in[:, t, :], op0=ALU.max, op1=ALU.add).then_inc(res_ready, 1)

            def row_stats(g, t):
                dve.wait_ge(res_ready, T * g + t + 1)
                nc.vector.bn_stats(stats[:, t, :], res[:, t, :]).then_inc(stats_ready, 1)

            def row_var(t):
                nc.vector.bn_aggr(mv[:, t, :], stats[:, t, :]).then_inc(var_ready, 1)

            def invert_std(n, first, end):
                tiles = slice(first, end)
                dve.wait_ge(std_ready, n)
                nc.vector.reciprocal(r0[:, tiles], std[:, tiles]).then_inc(r0_ready, 1)
                dve.wait_ge(r0_ready, n)
                nc.vector.tensor_tensor(r_sq[:, tiles], r0[:, tiles], r0[:, tiles], ALU.mult).then_inc(r_sq_ready, 1)
                dve.wait_ge(r_sq_ready, n)
                nc.vector.scalar_tensor_tensor(out=r_err[:, tiles], in0=mv[:, tiles, 1], scalar=EPS, in1=r_sq[:, tiles],
                                               op0=ALU.add, op1=ALU.mult).then_inc(r_err_ready, 1)
                dve.wait_ge(r_err_ready, n)
                nc.vector.tensor_scalar(r_fix[:, tiles], r_err[:, tiles], -0.5, 1.5, ALU.mult, ALU.add).then_inc(r_fix_ready, 1)
                dve.wait_ge(r_fix_ready, n)
                nc.vector.tensor_tensor(rstd[:, tiles], r0[:, tiles], r_fix[:, tiles], ALU.mult).then_inc(rstd_ready, 1)
                dve.wait_ge(rstd_ready, n)

            def normalise(t):
                nc.vector.tensor_scalar(o_sb[:, t, :], res[:, t, :], mv[:, t, 0:1], rstd[:, t:t + 1],
                                        ALU.subtract, ALU.mult).then_inc(o_ready, 1)

            def group(g):
                h = g - 1
                for q in range(Q):
                    to_mask(g, q)
                    if q == 2:
                        invert_deg(h)
                    if q == 5:
                        dve.wait_ge(stats_ready, T * (h + 1))
                    if q > 1:
                        sum_masks(g, q - 1)
                    if q == 3:
                        for t in range(T):
                            drain_acc(h, t, t < T - 1)
                        for t in range(2):
                            add_x(h, t, x_sb)
                    if q == 4:
                        for t in range(2, T):
                            add_x(h, t, x_sb)
                        for t in range(T):
                            row_stats(h, t)
                    if q == 5:
                        for t in range(T):
                            row_var(t)
                    if q == 7:
                        sum_masks(g, q)
                        invert_std(g, 0, T)
                        for t in range(T):
                            normalise(t)

            nc.vector.memset(warm[:], 0.0).then_inc(warm_set, 1)
            nc.vector.memset(ones[:], 1.0).then_inc(ones_set, 1)
            nc.vector.memset(one[:], 1.0).then_inc(consts_set, 1)
            nc.vector.memset(eps[:], EPS).then_inc(consts_set, 1)
            dve.wait_ge(b_landed, 16)
            dve.wait_ge(ones_set, 1)
            for k in range(2 * KD):
                nc.vector.tensor_scalar(b_wide[:, k, :], ones[:], b_in[:, k:k + 1], None, ALU.mult).then_inc(b_widened, 1)

            def split_lo(i):
                dve.wait_ge(hi_ready, i + 2 - i % 2)
                nc.vector.scalar_tensor_tensor(out=y[:, i, D:2 * D], in0=y_ps(i), scalar=unscale[:, i:i + 1],
                                               in1=y[:, i, 0:D], op0=ALU.mult, op1=ALU.subtract).then_inc(lo_ready, 1)

            for m in range(NT // 2):
                two = slice(2 * m, 2 * m + 2)
                if m % 2 == 0:
                    to_mask(0, m // 2)
                dve.wait_ge(y_product, m + 1)
                nc.vector.tensor_reduce(rowmax[:, two], yz[m % 3][:].rearrange("p (a n) -> p a n", a=2), AX.X,
                                        ALU.max, apply_absolute_value=True).then_inc(rowmax_ready, 1)
                if m:
                    split_lo(2 * m - 2)
                dve.wait_ge(rowmax_ready, m + 1)
                nc.vector.tensor_scalar(power[:, two].bitcast(I32), rowmax[:, two].bitcast(I32), EXPONENT, None,
                                        ALU.bitwise_and).then_inc(power_ready, 1)
                if m:
                    split_lo(2 * m - 1)
                dve.wait_ge(power_ready, m + 1)
                nc.vector.tensor_scalar(scale[:, two], power[:, two], LEAST, TOP, ALU.max,
                                        ALU.mult).then_inc(scale_ready, 1)
                dve.wait_ge(scale_ready, m + 1)
                nc.vector.reciprocal(unscale[:, two], scale[:, two]).then_inc(unscale_ready, 1)
                if m % 2 and m // 2:
                    sum_masks(0, m // 2)
                if m == 1:
                    dve.wait_ge(b_product, 1)
                    dve.wait_ge(bc_landed, 16)
                    nc.vector.tensor_tensor(bias[:], acc[2][:, 0:D], bc[:], ALU.add).then_inc(bias_ready, 1)
            split_lo(NT - 2)
            split_lo(NT - 1)

            with dve.Fori(1, G) as g:
                group(g)
            h = G - 1
            invert_deg(h)
            for t in range(T):
                drain_acc(h, t, True)
                add_x(h, t, x_last)
                row_stats(h, t)
                dve.wait_ge(stats_ready, T * h + t + 1)
                row_var(t)
                invert_std(G + t, t, t + 1)
                if t == 0:
                    dve.wait_ge(out_stored, 16 * h)
                normalise(t)

        @block.tensor
        def _(pe):
            def fold(dst, w, done):
                for a in range(KD):
                    for k in range(KD):
                        last = nc.tensor.matmul(dst[:, a * D:(a + 1) * D], w[:, k, a * P:(a + 1) * P], w[:, KD + k, :],
                                                start=(k == 0), stop=(k == KD - 1))
                last.then_inc(done, 1)

            def quad_products(g, q, tiles):
                pe.wait_ge(smask_ready, Q * g + q + 1)
                for t in tiles:
                    if q == 0 and not (isinstance(g, int) and g == 0):
                        pe.wait_ge(pre_ready, T * (g - 1) + t + 1)
                    for j in range(T):
                        last = nc.tensor.matmul(acc[t][:], smask[:, q % RING, j, t * P:(t + 1) * P],
                                                y[:, T * q + j, :], start=(q == 0 and j == 0),
                                                stop=(q == Q - 1 and j == T - 1))
                    if t == T - 1:
                        last.then_inc(quad_done, 1)
                    elif q == Q - 1:
                        last.then_inc(acc_done, 1)

            def degrees(g):
                pe.wait_ge(msum_ready, (Q - 1) * (g + 1))
                if not (isinstance(g, int) and g == 0):
                    pe.wait_ge(deg1_ready, g)
                for t in range(T):
                    for j in range(T):
                        last = nc.tensor.matmul(deg_ps[:, t:t + 1], msum[:, j, t * P:(t + 1) * P], one[:, 0:1],
                                                start=(j == 0), stop=(j == T - 1))
                last.then_inc(deg_done, 1)

            def z_product(g, t, src):
                for k in range(KD):
                    last = nc.tensor.matmul(z_ps(t), src[:, k * GROUP + t * P:k * GROUP + (t + 1) * P], ws[:, k, :],
                                            start=(k == 0), stop=(k == KD - 1))
                last.then_inc(z_done, 1)

            def quad_and_z(g, q):
                quad_products(g, q, range(T))
                if q < T:
                    if q == 0:
                        pe.wait_ge(xt_cur_ready, g)
                    pe.wait_ge(z_copied, T * g + q - 1)
                    z_product(g, q, xt_cur)

            pe.wait_ge(warm_set, 1)
            for _ in range(WARM):
                nc.tensor.matmul(acc[3][:], warm[:, 0:P], warm[:], start=True, stop=True)
            pe.wait_ge(wn_landed, 16)
            fold(acc[0], wn_in, wn_product)
            pe.wait_ge(ws_landed, 16)
            fold(acc[1], ws_in, ws_product)

            y_ahead = 3
            for m in range(NT // 2 + y_ahead):
                if m < NT // 2:
                    if m == 0:
                        pe.wait_ge(wn_ready, 1)
                    if m % 2 == 0:
                        pe.wait_ge(xt_landed[m // 2], 16)
                    if m >= 3:
                        pe.wait_ge(lo_ready, 2 * m - 4)
                    for i in (2 * m, 2 * m + 1):
                        for k in range(KD):
                            at = k * GROUP + (i % T) * P
                            last = nc.tensor.matmul(y_ps(i), xt[:, i // T, at:at + P], wn[:, k, :],
                                                    start=(k == 0), stop=(k == KD - 1))
                    last.then_inc(y_product, 1)
                elif m < NT // 2 + 2:
                    if m == NT // 2:
                        pe.wait_ge(ws_ready, 1)
                    for t in (2 * (m - NT // 2), 2 * (m - NT // 2) + 1):
                        if t < 2:
                            pe.wait_ge(lo_ready, NT - T + 2 * t)
                        else:
                            pe.wait_ge(z_copied, t - 1)
                        z_product(0, t, xt[:, 0, :])
                if m == 0:
                    pe.wait_ge(b_widened, 2 * KD)
                    for k in range(2 * KD):
                        w = ws_in if k < KD else wn_in
                        last = nc.tensor.matmul(acc[2][:, 0:D], b_wide[:, k, :], w[:, KD + k % KD, :],
                                                start=(k == 0), stop=(k == 2 * KD - 1))
                    last.then_inc(b_product, 1)
                if m >= y_ahead:
                    unit = m - y_ahead
                    if unit == 0:
                        pe.wait_ge(bias_ready, 1)
                        pe.wait_ge(ws_ready, 1)
                    if unit % 2 == 0:
                        pe.wait_ge(lo_ready, 2 * unit + T)
                    if unit == 2 * (Q - 1):
                        degrees(0)
                    quad_products(0, unit // 2, (0, 1) if unit % 2 == 0 else (2, 3))

            with pe.Fori(1, G - 1) as g:
                for q in range(Q):
                    if q == Q - 2:
                        degrees(g)
                    quad_and_z(g, q)

            g = G - 1
            for q in range(Q - RING):
                quad_and_z(g, q)
            for t in range(T):
                for q in range(Q - RING, Q):
                    if t == 0:
                        pe.wait_ge(smask_ready, Q * g + q + 1)
                    for j in range(T):
                        last = nc.tensor.matmul(acc[t][:], smask[:, q % RING, j, t * P:(t + 1) * P],
                                                y[:, T * q + j, :], start=False, stop=(q == Q - 1 and j == T - 1))
                last.then_inc(acc_done, 1)
                if t == 0:
                    degrees(g)


def kernel(x, adj, L0_gnn_W_self, L0_gnn_b_self, L0_gnn_W_nb, L0_gnn_b_nb, L0_gnn_W_comb, L0_gnn_b_comb):
    import numpy as np
    import concourse.bacc as bacc
    from concourse.bass_utils import run_bass_kernel_spmd

    def rows(w):
        w = np.asarray(w)
        return w.reshape(KD, P, -1).transpose(1, 0, 2)

    x, adj = np.asarray(x), np.asarray(adj)
    wc = np.asarray(L0_gnn_W_comb)
    ins = {
        "adj_t": np.ascontiguousarray(adj.reshape(G, P, T, Q, P, T).transpose(0, 3, 4, 5, 2, 1).reshape(G, Q, P, T, GROUP)),
        "x_rows": np.ascontiguousarray(x.reshape(G, P, T, D)),
        "x_t": np.ascontiguousarray(x.reshape(Q, P, T, KD, P).transpose(0, 4, 3, 2, 1).reshape(Q, P, KD * GROUP)),
        "w_nb": np.ascontiguousarray(np.concatenate([rows(np.asarray(L0_gnn_W_nb).T), rows(wc[D:])], axis=1)),
        "w_self": np.ascontiguousarray(np.concatenate([rows(np.asarray(L0_gnn_W_self).T), rows(wc[:D])], axis=1)),
        "b_cols": np.ascontiguousarray(np.concatenate([np.asarray(L0_gnn_b_self).reshape(KD, P), np.asarray(L0_gnn_b_nb).reshape(KD, P)]).T),
        "b_comb": np.ascontiguousarray(np.broadcast_to(np.asarray(L0_gnn_b_comb), (P, D))),
    }
    nc = bacc.Bacc("TRN2", target_bir_lowering=False, num_devices=1)
    aps = {name: nc.dram_tensor(name, a.shape, mybir.dt.from_np(a.dtype), kind="ExternalInput").ap()
           for name, a in ins.items()}
    out = nc.dram_tensor("out", (G, P, T, D), F32, kind="ExternalOutput").ap()
    gnn_layer(nc, out=out, **aps)
    r = run_bass_kernel_spmd(nc, [ins], core_ids=[0])
    return r.results[0]["out"].reshape(N, D)
```

```python
from contextlib import ExitStack

import concourse.bass as bass
from concourse import mybir

F32 = mybir.dt.float32
F16 = mybir.dt.float16
BF16 = mybir.dt.bfloat16
I32 = mybir.dt.int32
ALU = mybir.AluOpType
ACT = mybir.ActivationFunctionType
AX = mybir.AxisListType

P = 128
N = 4096
D = 256
KD = D // P
T = 4
GROUP = T * P
G = N // GROUP
Q = N // GROUP
NT = N // P
SUMS = Q - 1 + 2
RING = 4
WARM = 7
EPS = 1e-5
EXPONENT = 0x7F800000
TOP = 2.0 ** -14
LEAST = 2.0 ** -98



def gnn_layer(nc, adj_t, x_rows, x_t, w_nb, w_self, b_cols, b_comb, out):
    with ExitStack() as ctx:
        def sb(name, shape, dt):
            return ctx.enter_context(nc.sbuf_tensor(name, shape, dt))

        def psum(name):
            return ctx.enter_context(nc.psum_tensor(name, [P, 512], F32))

        def sem(name):
            return ctx.enter_context(nc.semaphore(name))

        adj_sb = sb("adj_sb", [P, RING, T, GROUP], I32)
        mask = sb("mask", [P, RING, T, GROUP], BF16)
        smask = sb("smask", [P, RING, T, GROUP], BF16)
        msum = sb("msum", [P, T, GROUP], BF16)
        y = sb("y", [P, NT, 2 * D], F16)
        xt = sb("xt", [P, Q, KD * GROUP], F32)
        xt_cur = sb("xt_cur", [P, KD * GROUP], F32)
        x_sb = sb("x_sb", [P, T, D], F32)
        wn_in = sb("wn_in", [P, 2 * KD, D], F32)
        ws_in = sb("ws_in", [P, 2 * KD, D], F32)
        b_in = sb("b_in", [P, 2 * KD], F32)
        b_rows = sb("b_rows", [P, D], F32)
        bc = sb("bc", [P, D], F32)
        bias = sb("bias", [P, D], F32)
        wn = sb("wn", [P, KD, D], F32)
        ws = sb("ws", [P, KD, D], F32)
        ones = sb("ones", [P, P], F32)
        one = sb("one", [P, 2], BF16)
        eps = sb("eps", [P, 1], F32)
        rowmax = sb("rowmax", [P, NT], F32)
        power = sb("power", [P, NT], F32)
        scale = sb("scale", [P, NT], F32)
        unscale = sb("unscale", [P, NT], F32)
        z_sb = sb("z_sb", [P, T, D], F32)
        zb = sb("zb", [P, T, D], F32)
        deg1 = sb("deg1", [P, T], F32)
        rdeg = sb("rdeg", [P, T], F32)
        half = sb("half", [P, T, D], F32)
        pre = sb("pre", [P, T, D], F32)
        res = sb("res", [P, T, D], F32)
        stats = sb("stats", [P, T, 6], F32)
        mv = sb("mv", [P, T, 2], F32)
        std = sb("std", [P, T], F32)
        r0 = sb("r0", [P, T], F32)
        r_sq = sb("r_sq", [P, T], F32)
        r_err = sb("r_err", [P, T], F32)
        r_fix = sb("r_fix", [P, T], F32)
        rstd = sb("rstd", [P, T], F32)
        x_last = sb("x_last", [P, T, D], F32)
        o_sb = sb("o_sb", [P, T, D], F32)
        warm = sb("warm", [P, 512], BF16)

        acc = [psum(f"acc{t}") for t in range(T)]
        yz = [psum(f"yz{b}") for b in range(3)]
        deg_ps = psum("deg_ps")

        adj_landed = [sem(f"adj_landed{s}") for s in range(RING)]
        xt_landed = [sem(f"xt_landed{q}") for q in range(Q)]
        x_landed = sem("x_landed")
        x_last_landed = sem("x_last_landed")
        wn_landed = sem("wn_landed")
        ws_landed = sem("ws_landed")
        b_landed = sem("b_landed")
        bc_landed = sem("bc_landed")
        out_stored = sem("out_stored")
        last_stored = sem("last_stored")
        warm_set = sem("warm_set")
        ones_set = sem("ones_set")
        consts_set = sem("consts_set")
        b_added = sem("b_added")
        wn_product = sem("wn_product")
        ws_product = sem("ws_product")
        b_product = sem("b_product")
        wn_ready = sem("wn_ready")
        ws_ready = sem("ws_ready")
        bias_ready = sem("bias_ready")
        y_product = sem("y_product")
        rowmax_ready = sem("rowmax_ready")
        power_ready = sem("power_ready")
        scale_ready = sem("scale_ready")
        unscale_ready = sem("unscale_ready")
        hi_ready = sem("hi_ready")
        lo_ready = sem("lo_ready")
        mask_ready = sem("mask_ready")
        smask_ready = sem("smask_ready")
        quad_done = sem("quad_done")
        acc_done = sem("acc_done")
        msum_ready = sem("msum_ready")
        deg_done = sem("deg_done")
        xt_cur_ready = sem("xt_cur_ready")
        z_done = sem("z_done")
        z_copied = sem("z_copied")
        zb_ready = sem("zb_ready")
        deg1_ready = sem("deg1_ready")
        rdeg_ready = sem("rdeg_ready")
        half_ready = sem("half_ready")
        pre_ready = sem("pre_ready")
        res_ready = sem("res_ready")
        stats_ready = sem("stats_ready")
        var_ready = sem("var_ready")
        std_ready = sem("std_ready")
        r0_ready = sem("r0_ready")
        r_sq_ready = sem("r_sq_ready")
        r_err_ready = sem("r_err_ready")
        r_fix_ready = sem("r_fix_ready")
        rstd_ready = sem("rstd_ready")
        o_ready = sem("o_ready")

        def y_ps(i):
            return yz[(i // 2) % 3][:, (i % 2) * D:(i % 2 + 1) * D]

        def z_ps(t):
            return yz[1 + t % 2][:, 0:D]

        block = ctx.enter_context(nc.Block())

        @block.sync
        def _(sp):
            def load_adj(g, q):
                if not (isinstance(g, int) and g == 0 and q < RING):
                    sp.wait_ge(mask_ready, Q * g + q + 1 - RING)
                sp.dma_start(adj_sb[:, q % RING, :, :], adj_t[g, q]).then_inc(adj_landed[q % RING], 16)

            def load_xt(q):
                sp.dma_start(xt[:, q, :], x_t[q]).then_inc(xt_landed[q], 16)

            sp.dma_start(wn_in[:], w_nb).then_inc(wn_landed, 16)
            sp.dma_start(ws_in[:], w_self).then_inc(ws_landed, 16)
            sp.dma_start(b_in[:], b_cols).then_inc(b_landed, 16)
            load_xt(0)
            load_adj(0, 0)
            sp.dma_start(bc[:], b_comb).then_inc(bc_landed, 16)
            load_xt(1)
            load_adj(0, 1)
            load_xt(2)
            load_xt(3)
            load_adj(0, 2)
            load_xt(4)
            load_xt(5)
            load_adj(0, 3)
            load_xt(6)
            load_xt(7)
            for q in range(4, Q):
                load_adj(0, q)
            sp.dma_start(x_last[:], x_rows[G - 1]).then_inc(x_last_landed, 16)
            with sp.Fori(1, G) as g:
                for q in range(Q):
                    load_adj(g, q)
            for t in range(T):
                sp.wait_ge(o_ready, T * (G - 1) + t + 1)
                sp.dma_start(out[G - 1, :, t, :], o_sb[:, t, :]).then_inc(last_stored, 16)
            sp.wait_ge(last_stored, 16 * T)

        @block.gpsimd
        def _(pool):
            def add_bias(g):
                for t in range(T):
                    pool.wait_ge(z_copied, T * g + t + 1)
                    if not (isinstance(g, int) and g == 0):
                        pool.wait_ge(pre_ready, T * (g - 1) + t + 1)
                    nc.gpsimd.tensor_tensor(zb[:, t, :], z_sb[:, t, :], bias[:], ALU.add).then_inc(zb_ready, 1)

            for q in range(Q):
                pool.wait_ge(xt_landed[q], 16)
            pool.dma_start(x_sb[:], x_rows[0]).then_inc(x_landed, 16)
            pool.wait_ge(bias_ready, 1)
            add_bias(0)
            def group(g):
                pool.wait_ge(z_done, T * g)
                nc.gpsimd.tensor_copy(xt_cur[:, :], xt[:, bass.ds(g, 1), :].rearrange("p a n -> p (a n)")).then_inc(xt_cur_ready, 1)
                add_bias(g)
                pool.wait_ge(o_ready, T * g)
                pool.dma_start(out[bass.ds(g - 1, 1)].rearrange("a p t n -> p (a t) n"), o_sb[:]).then_inc(out_stored, 16)

            with pool.Fori(1, G - 1) as g:
                group(g)
                pool.wait_ge(out_stored, 16 * g)
                pool.dma_start(x_sb[:], x_rows[bass.ds(g, 1)].rearrange("a p t n -> p (a t) n")).then_inc(x_landed, 16)
            group(G - 1)
            pool.wait_ge(out_stored, 16 * (G - 1))

        @block.scalar
        def _(act):
            def scale_mask(g, q, tiles):
                act.wait_ge(mask_ready, Q * g + q + 1)
                if not (isinstance(g, int) and g == 0 and q < RING):
                    act.wait_ge(quad_done, Q * g + q + 1 - RING)
                for j in tiles:
                    last = nc.scalar.activation(smask[:, q % RING, j, :], mask[:, q % RING, j, :], ACT.Copy,
                                                scale=scale[:, T * q + j:T * q + j + 1])
                if tiles[-1] == T - 1:
                    last.then_inc(smask_ready, 1)

            def copy_z(g, t):
                act.wait_ge(z_done, T * g + t + 1)
                if not (isinstance(g, int) and g == 0):
                    act.wait_ge(zb_ready, T * (g - 1) + t + 1)
                nc.scalar.activation(z_sb[:, t, :], z_ps(t), ACT.Copy).then_inc(z_copied, 1)

            def std_of(g, first, end):
                act.wait_ge(var_ready, T * g + end)
                nc.scalar.activation(std[:, first:end], mv[:, first:end, 1], ACT.Sqrt, bias=eps[:]).then_inc(std_ready, 1)

            def group(g):
                for q in range(Q):
                    scale_mask(g, q, range(T))
                    if 3 <= q < 3 + T:
                        copy_z(g, q - 3)
                    if q == 5:
                        std_of(g - 1, 0, T)

            act.wait_ge(consts_set, 2)
            nc.scalar.activation(std[:, 0:1], eps[:], ACT.Sqrt)
            act.wait_ge(wn_product, 1)
            nc.scalar.activation(wn[:], acc[0][:].rearrange("p (k n) -> p k n", k=KD), ACT.Copy).then_inc(wn_ready, 1)
            for m in range(NT // 2):
                act.wait_ge(unscale_ready, m + 1)
                for i in (2 * m, 2 * m + 1):
                    nc.scalar.activation(y[:, i, 0:D], y_ps(i), ACT.Copy,
                                         scale=unscale[:, i:i + 1]).then_inc(hi_ready, 1)
                scale_mask(0, m // 2, range(2 * (m % 2), 2 * (m % 2) + 2))
                if m == 1:
                    act.wait_ge(ws_product, 1)
                    nc.scalar.activation(ws[:], acc[3][:].rearrange("p (k n) -> p k n", k=KD), ACT.Copy).then_inc(ws_ready, 1)
            for t in range(T):
                copy_z(0, t)
            with act.Fori(1, G) as g:
                group(g)
            for t in range(T):
                std_of(G - 1, t, t + 1)

        @block.vector
        def _(dve):
            def to_mask(g, q):
                dve.wait_ge(adj_landed[q % RING], 16 * ((Q // RING) * g + q // RING + 1))
                if not (isinstance(g, int) and g == 0 and q < RING):
                    dve.wait_ge(smask_ready, Q * g + q + 1 - RING)
                nc.vector.tensor_scalar(mask[:, q % RING, :, :], adj_sb[:, q % RING, :, :], 0.0, None,
                                        ALU.is_gt).then_inc(mask_ready, 1)

            def sum_masks(g, q):
                dve.wait_ge(mask_ready, Q * g + q + 1)
                if q == 1:
                    if not (isinstance(g, int) and g == 0):
                        dve.wait_ge(deg_done, g)
                    first = mask[:, 0, :, :]
                else:
                    dve.wait_ge(msum_ready, SUMS * g + q - 1)
                    first = msum[:, :, :]
                nc.vector.tensor_tensor(msum[:, :, :], first, mask[:, q % RING, :, :],
                                        ALU.add).then_inc(msum_ready, 1)

            def fold_sum(g, step):
                n = T // 2 >> step
                dve.wait_ge(msum_ready, SUMS * g + Q - 1 + step)
                nc.vector.tensor_tensor(msum[:, 0:n, :], msum[:, 0:n, :], msum[:, n:2 * n, :],
                                        ALU.add).then_inc(msum_ready, 1)

            def invert_deg(g):
                dve.wait_ge(deg_done, g + 1)
                nc.vector.tensor_scalar(deg1[:], deg_ps[:, 0:T], 1.0, None, ALU.max).then_inc(deg1_ready, 1)
                dve.wait_ge(deg1_ready, g + 1)
                nc.vector.reciprocal(rdeg[:], deg1[:]).then_inc(rdeg_ready, 1)

            def drain_hi(g, t, own_count):
                dve.wait_ge(rdeg_ready, g + 1)
                dve.wait_ge(zb_ready, T * g + t + 1)
                if own_count:
                    dve.wait_ge(acc_done, (T - 1) * g + t + 1)
                else:
                    dve.wait_ge(quad_done, Q * (g + 1))
                nc.vector.scalar_tensor_tensor(out=half[:, t, :], in0=acc[t][:, 0:D], scalar=rdeg[:, t:t + 1],
                                               in1=zb[:, t, :], op0=ALU.mult, op1=ALU.add).then_inc(half_ready, 1)

            def drain_lo(g, t):
                dve.wait_ge(half_ready, T * g + t + 1)
                nc.vector.scalar_tensor_tensor(out=pre[:, t, :], in0=acc[t][:, D:2 * D], scalar=rdeg[:, t:t + 1],
                                               in1=half[:, t, :], op0=ALU.mult, op1=ALU.add).then_inc(pre_ready, 1)

            def add_x(g, t, x_in):
                if t == 0:
                    if x_in is x_last:
                        dve.wait_ge(x_last_landed, 16)
                    else:
                        dve.wait_ge(x_landed, 16 * (g + 1))
                dve.wait_ge(pre_ready, T * g + t + 1)
                nc.vector.scalar_tensor_tensor(out=res[:, t, :], in0=pre[:, t, :], scalar=0.0,
                                               in1=x_in[:, t, :], op0=ALU.max, op1=ALU.add).then_inc(res_ready, 1)

            def row_stats(g, t):
                dve.wait_ge(res_ready, T * g + t + 1)
                nc.vector.bn_stats(stats[:, t, :], res[:, t, :]).then_inc(stats_ready, 1)

            def row_var(t):
                nc.vector.bn_aggr(mv[:, t, :], stats[:, t, :]).then_inc(var_ready, 1)

            def rstd_start(n, tiles):
                dve.wait_ge(std_ready, n)
                nc.vector.reciprocal(r0[:, tiles], std[:, tiles]).then_inc(r0_ready, 1)

            def rstd_square(n, tiles):
                dve.wait_ge(r0_ready, n)
                nc.vector.tensor_tensor(r_sq[:, tiles], r0[:, tiles], r0[:, tiles], ALU.mult).then_inc(r_sq_ready, 1)

            def rstd_error(n, tiles):
                dve.wait_ge(r_sq_ready, n)
                nc.vector.scalar_tensor_tensor(out=r_err[:, tiles], in0=mv[:, tiles, 1], scalar=EPS, in1=r_sq[:, tiles],
                                               op0=ALU.add, op1=ALU.mult).then_inc(r_err_ready, 1)

            def rstd_factor(n, tiles):
                dve.wait_ge(r_err_ready, n)
                nc.vector.tensor_scalar(r_fix[:, tiles], r_err[:, tiles], -0.5, 1.5, ALU.mult, ALU.add).then_inc(r_fix_ready, 1)

            def rstd_finish(n, tiles):
                dve.wait_ge(r_fix_ready, n)
                nc.vector.tensor_tensor(rstd[:, tiles], r0[:, tiles], r_fix[:, tiles], ALU.mult).then_inc(rstd_ready, 1)

            def normalise(n, t):
                dve.wait_ge(rstd_ready, n)
                nc.vector.tensor_scalar(o_sb[:, t, :], res[:, t, :], mv[:, t, 0:1], rstd[:, t:t + 1],
                                        ALU.subtract, ALU.mult).then_inc(o_ready, 1)

            def group(g):
                h = g - 1
                for q in range(Q):
                    to_mask(g, q)
                    if q == 2:
                        invert_deg(h)
                    if q == 5:
                        dve.wait_ge(stats_ready, T * (h + 1))
                    if q > 3:
                        sum_masks(g, q - 1)
                    if q == 3:
                        for t in range(T):
                            drain_hi(h, t, t < T - 1)
                            drain_lo(h, t)
                        sum_masks(g, 1)
                        sum_masks(g, 2)
                        for t in range(2):
                            add_x(h, t, x_sb)
                    if q == 4:
                        for t in range(2, T):
                            add_x(h, t, x_sb)
                        for t in range(T):
                            row_stats(h, t)
                    if q == 5:
                        for t in range(T):
                            row_var(t)
                    if q == 7:
                        four = slice(0, T)
                        rstd_start(g, four)
                        sum_masks(g, q)
                        rstd_square(g, four)
                        rstd_error(g, four)
                        fold_sum(g, 0)
                        rstd_factor(g, four)
                        rstd_finish(g, four)
                        fold_sum(g, 1)
                        for t in range(T):
                            normalise(g, t)

            nc.vector.memset(warm[:], 0.0).then_inc(warm_set, 1)
            nc.vector.memset(ones[:], 1.0).then_inc(ones_set, 1)
            nc.vector.memset(one[:], 1.0).then_inc(consts_set, 1)
            nc.vector.memset(eps[:], EPS).then_inc(consts_set, 1)
            dve.wait_ge(b_landed, 16)
            dve.wait_ge(ws_landed, 16)
            nc.vector.tensor_scalar(b_rows[:], ws_in[:, KD, :], b_in[:, 0:1], None, ALU.mult).then_inc(b_added, 1)
            dve.wait_ge(wn_landed, 16)
            for k in range(1, 2 * KD):
                w = ws_in if k < KD else wn_in
                dve.wait_ge(b_added, k)
                nc.vector.scalar_tensor_tensor(out=b_rows[:], in0=w[:, KD + k % KD, :], scalar=b_in[:, k:k + 1],
                                               in1=b_rows[:], op0=ALU.mult, op1=ALU.add).then_inc(b_added, 1)

            def split_lo(i):
                dve.wait_ge(hi_ready, i + 2 - i % 2)
                nc.vector.scalar_tensor_tensor(out=y[:, i, D:2 * D], in0=y_ps(i), scalar=unscale[:, i:i + 1],
                                               in1=y[:, i, 0:D], op0=ALU.mult, op1=ALU.subtract).then_inc(lo_ready, 1)

            for m in range(NT // 2):
                two = slice(2 * m, 2 * m + 2)
                dve.wait_ge(y_product, m + 1)
                nc.vector.tensor_reduce(rowmax[:, two], yz[m % 3][:].rearrange("p (a n) -> p a n", a=2), AX.X,
                                        ALU.max, apply_absolute_value=True).then_inc(rowmax_ready, 1)
                dve.wait_ge(rowmax_ready, m + 1)
                nc.vector.tensor_scalar(power[:, two].bitcast(I32), rowmax[:, two].bitcast(I32), EXPONENT, None,
                                        ALU.bitwise_and).then_inc(power_ready, 1)
                dve.wait_ge(power_ready, m + 1)
                nc.vector.tensor_scalar(scale[:, two], power[:, two], LEAST, TOP, ALU.max,
                                        ALU.mult).then_inc(scale_ready, 1)
                dve.wait_ge(scale_ready, m + 1)
                nc.vector.reciprocal(unscale[:, two], scale[:, two]).then_inc(unscale_ready, 1)
                if m == 0:
                    to_mask(0, 0)
                if m % 2 and m // 2 + 1 < Q:
                    to_mask(0, m // 2 + 1)
                if m % 2 == 0 and m > 2:
                    sum_masks(0, m // 2 - 1)
                if m == NT // 2 - 1:
                    sum_masks(0, Q - 1)
                split_lo(2 * m)
                split_lo(2 * m + 1)
                if m == 4:
                    dve.wait_ge(b_product, 1)
                    dve.wait_ge(bc_landed, 16)
                    nc.vector.tensor_tensor(bias[:], deg_ps[:, 0:D], bc[:], ALU.add).then_inc(bias_ready, 1)
            fold_sum(0, 0)
            fold_sum(0, 1)

            with dve.Fori(1, G) as g:
                group(g)
            h = G - 1
            invert_deg(h)
            for t in range(T):
                before, n = slice(t - 1, t), G + t - 1
                drain_hi(h, t, True)
                if t:
                    rstd_start(n, before)
                drain_lo(h, t)
                if t:
                    rstd_square(n, before)
                add_x(h, t, x_last)
                if t:
                    rstd_error(n, before)
                row_stats(h, t)
                if t:
                    rstd_factor(n, before)
                dve.wait_ge(stats_ready, T * h + t + 1)
                row_var(t)
                if t:
                    rstd_finish(n, before)
                    if t == 1:
                        dve.wait_ge(out_stored, 16 * h)
                    normalise(n, t - 1)
            last_tile, n = slice(T - 1, T), G + T - 1
            rstd_start(n, last_tile)
            rstd_square(n, last_tile)
            rstd_error(n, last_tile)
            rstd_factor(n, last_tile)
            rstd_finish(n, last_tile)
            normalise(n, T - 1)

        @block.tensor
        def _(pe):
            def fold(dst, w, a):
                for k in range(KD):
                    last = nc.tensor.matmul(dst[:, a * D:(a + 1) * D], w[:, k, a * P:(a + 1) * P], w[:, KD + k, :],
                                            start=(k == 0), stop=(k == KD - 1))
                return last

            def quad_products(g, q, tiles):
                pe.wait_ge(smask_ready, Q * g + q + 1)
                for t in tiles:
                    if q == 0 and not (isinstance(g, int) and g == 0):
                        pe.wait_ge(pre_ready, T * (g - 1) + t + 1)
                    for j in range(T):
                        last = nc.tensor.matmul(acc[t][:], smask[:, q % RING, j, t * P:(t + 1) * P],
                                                y[:, T * q + j, :], start=(q == 0 and j == 0),
                                                stop=(q == Q - 1 and j == T - 1))
                    if t == T - 1:
                        last.then_inc(quad_done, 1)
                    elif q == Q - 1:
                        last.then_inc(acc_done, 1)

            def degrees(g):
                pe.wait_ge(msum_ready, SUMS * (g + 1))
                if not (isinstance(g, int) and g == 0):
                    pe.wait_ge(deg1_ready, g)
                for t in range(T):
                    last = nc.tensor.matmul(deg_ps[:, t:t + 1], msum[:, 0, t * P:(t + 1) * P], one[:, 0:1],
                                            start=True, stop=True)
                last.then_inc(deg_done, 1)

            def z_product(g, t, src):
                for k in range(KD):
                    last = nc.tensor.matmul(z_ps(t), src[:, k * GROUP + t * P:k * GROUP + (t + 1) * P], ws[:, k, :],
                                            start=(k == 0), stop=(k == KD - 1))
                last.then_inc(z_done, 1)

            def quad_and_z(g, q):
                quad_products(g, q, range(T))
                if q < T:
                    if q == 0:
                        pe.wait_ge(xt_cur_ready, g)
                    pe.wait_ge(z_copied, T * g + q - 1)
                    z_product(g, q, xt_cur)

            pe.wait_ge(warm_set, 1)
            for _ in range(WARM):
                nc.tensor.matmul(acc[3][:], warm[:, 0:P], warm[:], start=True, stop=True)
            pe.wait_ge(wn_landed, 16)
            fold(acc[0], wn_in, 0)
            fold(acc[0], wn_in, 1).then_inc(wn_product, 1)
            pe.wait_ge(ws_landed, 16)
            fold(acc[3], ws_in, 0)

            y_ahead = 3
            for m in range(NT // 2 + y_ahead):
                if m < NT // 2:
                    if m == 0:
                        pe.wait_ge(wn_ready, 1)
                    if m % 2 == 0:
                        pe.wait_ge(xt_landed[m // 2], 16)
                    if m >= 3:
                        pe.wait_ge(lo_ready, 2 * m - 4)
                    for i in (2 * m, 2 * m + 1):
                        for k in range(KD):
                            at = k * GROUP + (i % T) * P
                            last = nc.tensor.matmul(y_ps(i), xt[:, i // T, at:at + P], wn[:, k, :],
                                                    start=(k == 0), stop=(k == KD - 1))
                    last.then_inc(y_product, 1)
                elif m < NT // 2 + 2:
                    if m == NT // 2:
                        pe.wait_ge(ws_ready, 1)
                    for t in (2 * (m - NT // 2), 2 * (m - NT // 2) + 1):
                        if t < 2:
                            pe.wait_ge(lo_ready, NT - T + 2 * t)
                        else:
                            pe.wait_ge(z_copied, t - 1)
                        z_product(0, t, xt[:, 0, :])
                if m == 2:
                    fold(acc[3], ws_in, 1).then_inc(ws_product, 1)
                    pe.wait_ge(b_added, 2 * KD)
                    pe.wait_ge(ones_set, 1)
                    nc.tensor.matmul(deg_ps[:, 0:D], ones[:], b_rows[:], start=True, stop=True).then_inc(b_product, 1)
                if m >= y_ahead:
                    unit = m - y_ahead
                    if unit == 1:
                        pe.wait_ge(ws_ready, 1)
                    if unit % 2 == 0:
                        pe.wait_ge(lo_ready, 2 * unit + T)
                    if unit == 2 * (Q - 1):
                        pe.wait_ge(bias_ready, 1)
                        pe.wait_ge(consts_set, 2)
                        degrees(0)
                    quad_products(0, unit // 2, (0, 1) if unit % 2 == 0 else (2, 3))

            with pe.Fori(1, G - 1) as g:
                for q in range(Q):
                    if q == Q - 2:
                        degrees(g)
                    quad_and_z(g, q)

            g = G - 1
            for q in range(Q - RING):
                quad_and_z(g, q)
            for t in range(T):
                for q in range(Q - RING, Q):
                    if t == 0 and q == Q - 1:
                        degrees(g)
                    if t == 0:
                        pe.wait_ge(smask_ready, Q * g + q + 1)
                    for j in range(T):
                        last = nc.tensor.matmul(acc[t][:], smask[:, q % RING, j, t * P:(t + 1) * P],
                                                y[:, T * q + j, :], start=False, stop=(q == Q - 1 and j == T - 1))
                last.then_inc(acc_done, 1)


def kernel(x, adj, L0_gnn_W_self, L0_gnn_b_self, L0_gnn_W_nb, L0_gnn_b_nb, L0_gnn_W_comb, L0_gnn_b_comb):
    import numpy as np
    import concourse.bacc as bacc
    from concourse.bass_utils import run_bass_kernel_spmd

    def rows(w):
        w = np.asarray(w)
        return w.reshape(KD, P, -1).transpose(1, 0, 2)

    x, adj = np.asarray(x), np.asarray(adj)
    wc = np.asarray(L0_gnn_W_comb)
    ins = {
        "adj_t": np.ascontiguousarray(adj.reshape(G, P, T, Q, P, T).transpose(0, 3, 4, 5, 2, 1).reshape(G, Q, P, T, GROUP)),
        "x_rows": np.ascontiguousarray(x.reshape(G, P, T, D)),
        "x_t": np.ascontiguousarray(x.reshape(Q, P, T, KD, P).transpose(0, 4, 3, 2, 1).reshape(Q, P, KD * GROUP)),
        "w_nb": np.ascontiguousarray(np.concatenate([rows(np.asarray(L0_gnn_W_nb).T), rows(wc[D:])], axis=1)),
        "w_self": np.ascontiguousarray(np.concatenate([rows(np.asarray(L0_gnn_W_self).T), rows(wc[:D])], axis=1)),
        "b_cols": np.ascontiguousarray(np.concatenate([np.asarray(L0_gnn_b_self).reshape(KD, P), np.asarray(L0_gnn_b_nb).reshape(KD, P)]).T),
        "b_comb": np.ascontiguousarray(np.broadcast_to(np.asarray(L0_gnn_b_comb), (P, D))),
    }
    nc = bacc.Bacc("TRN2", target_bir_lowering=False, num_devices=1)
    aps = {name: nc.dram_tensor(name, a.shape, mybir.dt.from_np(a.dtype), kind="ExternalInput").ap()
           for name, a in ins.items()}
    out = nc.dram_tensor("out", (G, P, T, D), F32, kind="ExternalOutput").ap()
    gnn_layer(nc, out=out, **aps)
    r = run_bass_kernel_spmd(nc, [ins], core_ids=[0])
    return r.results[0]["out"].reshape(N, D)
```
